# Optimizing a Trainium2 kernel written in Bass

```python
import numpy as np
import jax
import jax.numpy as jnp

def _softmax(x, axis=-1):
    return jax.nn.softmax(x, axis=axis)

def _gelu(x):
    return jax.nn.gelu(x, approximate=True)

def _silu(x):
    return jax.nn.silu(x)

def _sigmoid(x):
    return jax.nn.sigmoid(x)

def _layernorm(x, axis=-1, eps=1e-05):
    m = jnp.mean(x, axis=axis, keepdims=True)
    v = jnp.var(x, axis=axis, keepdims=True)
    return (x - m) / jnp.sqrt(v + eps)

def _scatter_add(tgt, idx, src, axis=0):
    return tgt.at[idx].add(src)

def _segment_sum(src, seg, n):
    return jax.ops.segment_sum(src, seg, n)
kernel_name = 'mk_rec_standalone_d1_rec_r8_f362c4'

def setup_inputs(seed: int=0):
    np.random.seed(seed)
    _w = jnp.asarray

    def _rec_inputs():
        import jax
        import jax.numpy as jnp
        _rk = jax.random.key(seed)
        r_dense_features = -0.000520686 + 1.00062 * jax.random.normal(jax.random.fold_in(_rk, 1), (512, 512), jnp.float32)
        r_sparse_features = jax.random.randint(jax.random.fold_in(_rk, 2), (26, 512, 50), 0, 12500, jnp.int32)
        return (r_dense_features, r_sparse_features)
    r_dense_features, r_sparse_features = _rec_inputs()

    def _L0_rec_setup():
        import jax, jax.numpy as jnp
        import numpy as np
        NUM_TABLES = 26
        NUM_EMB = 12500
        EMB_DIM = 64
        DENSE_DIM = 512
        BATCH = 512
        BAG = 50
        HIDDEN_OUT = 512

        def _mlp(x, w1, b1, w2, b2):
            h = jax.nn.relu(x @ w1.T + b1)
            return jax.nn.relu(h @ w2.T + b2)
        key = jax.random.key(seed)
        ks = jax.random.split(key, 12)
        dense_features = jax.random.normal(ks[0], (BATCH, DENSE_DIM), dtype=jnp.float32)
        sparse_features = jax.random.randint(ks[1], (NUM_TABLES, BATCH, BAG), 0, NUM_EMB, dtype=jnp.int64)
        emb_tables = jax.random.normal(ks[2], (NUM_TABLES, NUM_EMB, EMB_DIM), dtype=jnp.float32) * 0.01
        d_w1 = jax.random.normal(ks[3], (DENSE_DIM, DENSE_DIM), dtype=jnp.float32) * (1.0 / np.sqrt(DENSE_DIM))
        d_b1 = jnp.zeros((DENSE_DIM,), dtype=jnp.float32)
        d_w2 = jax.random.normal(ks[4], (EMB_DIM, DENSE_DIM), dtype=jnp.float32) * (1.0 / np.sqrt(DENSE_DIM))
        d_b2 = jnp.zeros((EMB_DIM,), dtype=jnp.float32)
        feat_dim = EMB_DIM * NUM_TABLES + EMB_DIM
        o_w1 = jax.random.normal(ks[5], (HIDDEN_OUT, feat_dim), dtype=jnp.float32) * (1.0 / np.sqrt(feat_dim))
        o_b1 = jnp.zeros((HIDDEN_OUT,), dtype=jnp.float32)
        o_w2 = jax.random.normal(ks[6], (1, HIDDEN_OUT), dtype=jnp.float32) * (1.0 / np.sqrt(HIDDEN_OUT))
        o_b2 = jnp.zeros((1,), dtype=jnp.float32)
        return dict(dense_features=dense_features, sparse_features=sparse_features, emb_tables=emb_tables, d_w1=d_w1, d_b1=d_b1, d_w2=d_w2, d_b2=d_b2, o_w1=o_w1, o_b1=o_b1, o_w2=o_w2, o_b2=o_b2)
    _L0_rec_all = _L0_rec_setup()
    _L0_rec_in = {k: v for k, v in _L0_rec_all.items() if k in ('emb_tables', 'd_w1', 'd_b1', 'd_w2', 'd_b2', 'o_w1', 'o_b1', 'o_w2', 'o_b2')}
    del _L0_rec_all
    return {'r_dense_features': r_dense_features, 'r_sparse_features': r_sparse_features, 'L0_rec_emb_tables': _L0_rec_in['emb_tables'], 'L0_rec_d_w1': _L0_rec_in['d_w1'], 'L0_rec_d_b1': _L0_rec_in['d_b1'], 'L0_rec_d_w2': _L0_rec_in['d_w2'], 'L0_rec_d_b2': _L0_rec_in['d_b2'], 'L0_rec_o_w1': _L0_rec_in['o_w1'], 'L0_rec_o_b1': _L0_rec_in['o_b1'], 'L0_rec_o_w2': _L0_rec_in['o_w2'], 'L0_rec_o_b2': _L0_rec_in['o_b2']}

def reference(r_dense_features, r_sparse_features, L0_rec_emb_tables, L0_rec_d_w1, L0_rec_d_b1, L0_rec_d_w2, L0_rec_d_b2, L0_rec_o_w1, L0_rec_o_b1, L0_rec_o_w2, L0_rec_o_b2):
    import jax
    import jax.numpy as jnp

    def _L0_rec_ref(dense_features, sparse_features, emb_tables, d_w1, d_b1, d_w2, d_b2, o_w1, o_b1, o_w2, o_b2):
        import jax, jax.numpy as jnp
        import numpy as np
        NUM_TABLES = 26
        NUM_EMB = 12500
        EMB_DIM = 64
        DENSE_DIM = 512
        BATCH = 512
        BAG = 50
        HIDDEN_OUT = 512

        def _mlp(x, w1, b1, w2, b2):
            h = jax.nn.relu(x @ w1.T + b1)
            return jax.nn.relu(h @ w2.T + b2)
        dense_x = _mlp(dense_features, d_w1, d_b1, d_w2, d_b2)
        pooled = jax.vmap(lambda tbl, idx: jnp.take(tbl, idx, axis=0).sum(axis=1))(emb_tables, sparse_features)
        B = dense_features.shape[0]
        emb_x = jnp.transpose(pooled, (1, 0, 2)).reshape(B, -1)
        features = jnp.concatenate([dense_x, emb_x], axis=1)
        logits = _mlp(features, o_w1, o_b1, o_w2, o_b2)
        return logits
    y = _L0_rec_ref(r_dense_features, r_sparse_features, L0_rec_emb_tables, L0_rec_d_w1, L0_rec_d_b1, L0_rec_d_w2, L0_rec_d_b2, L0_rec_o_w1, L0_rec_o_b1, L0_rec_o_w2, L0_rec_o_b2)
    return y

_drawn_inputs = setup_inputs


def setup_inputs(seed=0):
    import zlib

    import numpy as np

    out = dict(_drawn_inputs(seed))
    spreads = {'L0_rec_d_b1': (0.0, 0.1), 'L0_rec_d_b2': (0.0, 0.1), 'L0_rec_o_b1': (0.0, 0.1)}
    factors = {}
    for name, (base, spread) in spreads.items():
        noise = np.random.default_rng([zlib.crc32(name.encode()), seed]).standard_normal(out[name].shape)
        drawn = base * np.exp(spread * noise) if base else spread * noise
        out[name] = jnp.asarray(drawn.astype(out[name].dtype))
    for name, factor in factors.items():
        out[name] = (out[name] * factor).astype(out[name].dtype)
    return out
```

```python
from contextlib import ExitStack

import concourse.bass as bass
from concourse import mybir


def embedding_bag_mlp_program(nc, dense_T, bag_index, gather_index, tables, d_w1T, d_b1, d_w2T, d_b2,
                              o_w1T, o_b1, o_w2T, o_b2, logits):
    fp32, bf16, i32 = mybir.dt.float32, mybir.dt.bfloat16, mybir.dt.int32
    ALU = mybir.AluOpType
    ACT = mybir.ActivationFunctionType
    AX = mybir.AxisListType

    P = 128
    ALL, V, E = tables.shape
    STEPS, G, _, GN = gather_index.shape
    T = ALL - G
    DD, B = dense_T.shape
    HID = o_w1T.shape[1]
    BAG = 50
    ROWS = -(-V // P)
    LAST = V - (P - 1) * ROWS
    HALF = P // 2
    SLOT = P
    NSLOT = B // SLOT
    PAIRS = SLOT // 2
    GROUP = 512 // ROWS
    CHUNK = 2 * GROUP
    GROUPS = [(q, min(GROUP, PAIRS - q)) for q in range(0, PAIRS, GROUP)]
    CHUNKS = [(q, min(CHUNK, PAIRS - q)) for q in range(0, PAIRS, CHUNK)]
    NC, NG = len(CHUNKS), len(GROUPS)
    NBUF = 4
    AHEAD = 3
    PIECES = 7
    W = ROWS * E
    PL = ROWS // PIECES
    PW = PL * E
    RES_AT = {(1, 0): 0, (1, 1): 1, (1, 3): 2, (1, 4): 3, (1, 6): 4, (2, 0): 5, (2, 2): 6}
    LO_AT = {(2, 3): 0, (2, 5): 1, (2, 6): 2, (3, 1): 3, (3, 2): 4, (3, 4): 5, (3, 5): 6}
    SUM_AT = {(1, 0): 0, (3, 0): 1}
    MAGIC = 1.5 * 2.0 ** 23
    KD, KH, KF = DD // P, HID // P, ALL * E // P
    GJ = GN // NSLOT
    assert ROWS % PIECES == 0 and T % 2 == 0 and NSLOT % 2 == 0 and NSLOT * NC % NBUF == 0
    assert NSLOT * NG % 2 == 0 and BAG <= HALF
    assert G == 4 and STEPS * GJ == BAG and STEPS == T // 2 - 1

    ctx = ExitStack()
    with ctx:
        def sb(name, shape, dt):
            return ctx.enter_context(nc.sbuf_tensor(name, shape, dt))

        def pb(name, shape, dt=fp32):
            return ctx.enter_context(nc.psum_tensor(name, shape, dt))

        def sem(name):
            return ctx.enter_context(nc.semaphore(name))

        both = [sb(f"table_and_residual{i}", [P, 2 * W + 1], fp32) for i in range(2)]
        counts = [sb(f"counts{i}", [P, SLOT * ROWS], bf16) for i in range(2)]
        oh_hi = [sb(f"onehot_hi{i}", [P, CHUNK, P], bf16) for i in range(NBUF)]
        oh_lo = [sb(f"onehot_lo{i}", [P, CHUNK, ROWS], bf16) for i in range(NBUF)]
        stage = sb("pooled_stage", [P, NSLOT, 2, E], fp32)
        g_pool = sb("gathered_pooled", [P, G // 2, NSLOT, 2, E], fp32)
        w_x = sb("weight_o1_rest", [P, 2, HID], fp32)
        idx = [sb(f"bag_index{i}", [P, B // 2], fp32) for i in range(2)]
        hi2 = [sb(f"hi_twice{i}", [P, B // 2, 2], bf16) for i in range(2)]
        lo2 = [sb(f"lo_twice{i}", [P, B // 2, 2], bf16) for i in range(2)]
        quot, hi_f = (sb(n, [P, B // 2], fp32) for n in ("quotient", "hi_float"))
        step_const = sb("step_constants", [P, 5], fp32)
        g_raw = [sb(f"gather_index{i}", [P, GN], i32) for i in range(2)]
        g_row = [sb(f"gather_row{i}", [P, GN], i32) for i in range(G)]
        g_base = sb("gather_base", [P, G, GN], i32)
        g_buf = [sb(f"gathered_rows{i}", [P, NSLOT, GJ, E], fp32) for i in range(2)]
        g_sum = [sb(f"gathered_sum{i}", [P, NSLOT, E], fp32) for i in range(2)]
        ramp = sb("ramp", [P, P], bf16)
        ident = sb("ident", [P, P], fp32)
        dense_x = sb("dense_x", [E, B], fp32)
        b_d1 = sb("bias_d1", [P, KH], fp32)
        b_d2 = sb("bias_d2", [E, 1], fp32)
        b_o1 = sb("bias_o1", [P, KH], fp32)
        b_o2 = sb("bias_o2", [1, 1], fp32)
        w_o2 = sb("weight_o2", [P, KH], fp32)
        out_row = hi_f[0:1, :], quot[0:1, :]

        tab = [x[:, 0:W] for x in both]
        res = [x[:, W + 1:2 * W + 1] for x in both]
        halves = [x[:, :].bitcast(bf16).rearrange("p (w h) -> p w h", h=2) for x in both]
        SHIFT = W // 2 + 1

        def three_parts(i, l):
            flat = both[i][:, :].bitcast(bf16)
            return bass.AP(flat.tensor, flat.offset + 2 * l * E + 1, [list(flat.ap[0]), [W + 1, 3], [2, E]])
        spill = nc.dram_tensor("pooled_spill", (T // 2 - 1, P, NSLOT, 2, E), fp32).ap()

        xT = res[1][:, 0:KD * B].rearrange("p (k n) -> p k n", k=KD)
        w_d1 = res[1][:, KD * B:KD * (B + HID)].rearrange("p (k n) -> p k n", k=KD)
        w_d2 = res[1][:, KD * (B + HID):KD * (B + HID) + KH * E].rearrange("p (k n) -> p k n", k=KH)
        h_d = counts[1][:, :].bitcast(fp32)[:, 0:KH * B].rearrange("p (k n) -> p k n", k=KH)
        back = tab[0][:, 0:(T - 2) * NSLOT * E].rearrange("p (u s e) -> p u s e", u=T // 2 - 1, s=NSLOT)
        KW = (ROWS * E) // HID
        w_a = res[0][:, 0:KW * HID].rearrange("p (k n) -> p k n", k=KW)
        h_o = res[1][:, 0:KH * B].rearrange("p (k n) -> p k n", k=KH)
        w_feat = [w_a[:, k, :] if k < KW else w_x[:, k - KW, :] for k in range(KF)]
        w_dense = w_x[0:E, KF - KW, :]
        LATE = T // 2 - 1
        EARLY = [k for k in range(KF) if k != LATE]
        feat = {k: counts[0][:, :].bitcast(fp32)[:, x * B:(x + 1) * B] for x, k in enumerate(EARLY)}
        feat[LATE] = counts[1][:, :].bitcast(fp32)[:, 0:B]
        assert KF - KW == 1 and len(EARLY) * B <= ROWS * E and len(EARLY) < NG

        def sums(k, s):
            if k < LATE:
                return back[:, k, s, :]
            pair = stage[:, s, :, :] if k == LATE else g_pool[:, k - LATE - 1, s, :, :]
            return pair.rearrange("p t e -> p (t e)")

        ps_cnt = [pb(f"ps_counts{i}", [P, 2, 512]) for i in range(2)]
        ps_acc = [pb(f"ps_pooled{i}", [P, 512]) for i in range(2)]
        ps_mlp = [pb(f"ps_mlp{i}", [P, 512]) for i in range(2)]

        constants = sem("constants")
        tails_zero = sem("tails_zero")
        table_loaded = [sem(f"table_loaded{i}") for i in range(2)]
        index_loaded = [sem(f"index_loaded{i}") for i in range(2)]
        index_steps = sem("index_steps")
        index_split = sem("index_split")
        onehot_ready = sem("onehot_ready")
        group_ready = sem("group_ready")
        counts_ready = sem("counts_ready")
        residual_ready = sem("residual_ready")
        parts_ready = sem("parts_ready")
        slot_done = sem("slot_done")
        acc_free = sem("acc_free")
        g_loaded = [sem(f"gather_index_loaded{i}") for i in range(2)]
        gathered = [sem(f"gathered{i}") for i in range(2)]
        rows_ready = sem("rows_ready")
        g_free = sem("gather_buffer_free")
        g_added = sem("gather_added")
        spilled = sem("spilled")
        stage_free = sem("stage_free")
        back_loaded = sem("sums_loaded_back")
        dense_loaded = sem("dense_loaded")
        weights_loaded = sem("weights_loaded")
        mlp_ready = sem("mlp_ready")
        mlp_used = sem("mlp_used")
        feat_ready = sem("feat_ready")
        feat_used = [sem(f"feat_used{i}") for i in range(2)]
        out_stored = sem("out_stored")

        GT, CT = NSLOT * NG, NSLOT * NC
        LOADS = 3 * 16
        LOOPS = T // 2 - 1

        def groups_before(s, c):
            return s * NG + min(2 * c, NG)

        block = ctx.enter_context(nc.Block())

        @block.sync
        def _(sp):
            def load_table(t, i):
                for p0, p1 in ((0, 112), (112, P - 1)):
                    sp.dma_start(tab[i][p0:p1, :],
                                 tables[t, p0 * ROWS:p1 * ROWS, :].rearrange("(p r) e -> p (r e)", r=ROWS)
                                 ).then_inc(table_loaded[i], 16)
                sp.dma_start(tab[i][P - 1:P, 0:LAST * E],
                             tables[t, (P - 1) * ROWS:V, :].rearrange("(p r) e -> p (r e)", p=1)
                             ).then_inc(table_loaded[i], 16)

            with nc.allow_non_contiguous_dma(reason="bias columns, once"):
                for dst, src in ((xT, dense_T.rearrange("(k p) n -> p k n", p=P)),
                                 (w_d1, d_w1T.rearrange("(k p) n -> p k n", p=P)),
                                 (w_d2, d_w2T.rearrange("(k p) n -> p k n", p=P)),
                                 (b_d1[:, :], d_b1.rearrange("(k p) -> p k", p=P)),
                                 (b_d2[:, :], d_b2.rearrange("(p n) -> p n", n=1)),
                                 (b_o1[:, :], o_b1.rearrange("(k p) -> p k", p=P)),
                                 (b_o2[:, :], o_b2.rearrange("(p n) -> p n", n=1)),
                                 (w_o2[:, :], o_w2T.rearrange("(k p) n -> p (k n)", p=P))):
                    sp.dma_start(dst, src).then_inc(dense_loaded, 16)

            for i in range(2):
                sp.wait_ge(tails_zero, i + 1)
                load_table(i, i)
            for dst, src in ((w_x[:, 0, :], o_w1T[E + KW * P:, :]), (w_dense, o_w1T[0:E, :])):
                sp.dma_start(dst, src).then_inc(weights_loaded, 16)

            def spill_sums(u, i):
                t = u * 2 + i
                sp.wait_ge(acc_free, t * NSLOT + (NSLOT + 2))
                sp.dma_start(spill[u, :, :, i, :], stage[:, :, i, :]).then_inc(spilled, 16)
                sp.wait_ge(spilled, t * 16 + 16)
                sp.sem_inc(stage_free, 1)

            with sp.Fori(0, LOOPS) as u:
                sp.wait_ge(slot_done, u * (2 * NSLOT) + NSLOT)
                load_table(u * 2 + 2, 0)
                spill_sums(u, 0)
                sp.wait_ge(slot_done, u * (2 * NSLOT) + 2 * NSLOT)
                load_table(u * 2 + 3, 1)
                spill_sums(u, 1)
            sp.wait_ge(slot_done, (T - 1) * NSLOT)
            sp.dma_start(back.rearrange("p u s e -> p u (s e)"), spill.rearrange("u p s t e -> p u (s t e)")
                         ).then_inc(back_loaded, 16)
            sp.dma_start(w_a, o_w1T[E:E + KW * P, :].rearrange("(k p) n -> p k n", p=P)).then_inc(weights_loaded, 16)
            sp.wait_ge(mlp_used, 2 * KH + 3)
            for h in range(2):
                sp.dma_start(logits[h * (B // 2):(h + 1) * (B // 2), :].rearrange("b n -> n b"), out_row[h]
                             ).then_inc(out_stored, 16)
            sp.wait_ge(out_stored, 32)

        @block.gpsimd
        def _(pool):
            nc.gpsimd.iota(ramp[:, :], pattern=[[1, P]], base=0, channel_multiplier=0,
                           allow_small_or_imprecise_dtypes=True).then_inc(constants, 1)
            nc.gpsimd.memset(ident[:, :], 0.0).then_inc(constants, 1)
            pool.wait_ge(constants, 2)
            nc.gpsimd.affine_select(out=ident[:, :], in_=ident[:, :], compare_op=ALU.not_equal, fill=1.0,
                                    base=0, pattern=[[-1, P]], channel_multiplier=1).then_inc(constants, 1)

            for c, v in enumerate((-(ROWS - 1) / 2.0, 1.0 / ROWS, MAGIC, -MAGIC, -float(ROWS))):
                nc.gpsimd.memset(step_const[:, c:c + 1], v)
            nc.gpsimd.iota(g_base[:, :, :], pattern=[[V, G], [0, GN]], base=T * V, channel_multiplier=0)
            pool.drain()

            def load_index(t, i):
                pool.dma_start(idx[i][:, :], bag_index[t, :, :]).then_inc(index_loaded[i], 16)

            def split_index(t, i, turn):
                one, two = [P, B // 2], [P, B // 2, 2]
                pool.wait_ge(index_loaded[i], turn * 16 + 16)
                if not (isinstance(t, int) and t < 1):
                    pool.wait_ge(index_split, t * 2)
                src, n = idx[i], t * 5
                for c, (dst, op) in enumerate(((quot, ALU.add), (hi_f, ALU.mult), (quot, ALU.add),
                                               (hi_f, ALU.add), (quot, ALU.mult))):
                    if c > 0:
                        pool.wait_ge(index_steps, n + c)
                    nc.gpsimd.tensor_tensor(dst[:, :], src[:, :], step_const[:, c:c + 1].broadcast_to(one), op
                                            ).then_inc(index_steps, 1)
                    src = dst
                if not (isinstance(t, int) and t < 2):
                    pool.wait_ge(onehot_ready, t * CT - CT)
                pool.wait_ge(index_steps, n + 5)
                nc.gpsimd.tensor_tensor(lo2[i][:, :, :], idx[i][:, :].unsqueeze(2).broadcast_to(two),
                                        quot[:, :].unsqueeze(2).broadcast_to(two), ALU.add
                                        ).then_inc(index_split, 1)
                nc.gpsimd.tensor_copy(hi2[i][:, :, :], hi_f[:, :].unsqueeze(2).broadcast_to(two)
                                      ).then_inc(index_split, 1)

            def load_gather_index(step, g):
                pool.dma_start(g_raw[g % 2][:, :], gather_index[step, g, :, :]).then_inc(g_loaded[g % 2], 16)

            def rows(step, g, tables_split):
                step, g = (step, g) if g < G else (step + 1, g - G)
                n = step * G + g
                if tables_split is not None:
                    pool.wait_ge(index_split, tables_split * 2)
                if not (isinstance(step, int) and n == 0):
                    pool.wait_ge(rows_ready, n)
                    pool.wait_ge(g_free, n)
                pool.wait_ge(g_loaded[g % 2], step * (8 * G) + (g // 2 + 1) * 16)
                nc.gpsimd.tensor_tensor(g_row[g][:, :], g_raw[g % 2][:, :], g_base[:, g, :], ALU.add
                                        ).then_inc(rows_ready, 1)

            def gather(step, g):
                h = g % 2
                for x in range(GN):
                    s_, j = divmod(x, GJ)
                    nc.gpsimd.indirect_dma_start(g_buf[h][:, s_, j, :], None, tables.rearrange("t v e -> (t v) e"),
                                                 bass.IndirectOffsetOnAxis(g_row[g][:, x:x + 1], 0)
                                                 ).then_inc(gathered[h], 16)

            def batch(step, g, tables_split=None, index=None, left=G):
                if g + 1 < left:
                    rows(step, g + 1, tables_split)
                else:
                    pool.wait_ge(rows_ready, STEPS * G)
                    pool.wait_ge(g_free, STEPS * G)
                if g + 2 < left:
                    load_gather_index(*((step, g + 2) if g + 2 < G else (step + 1, g + 2 - G)))
                if index is not None:
                    load_index(*index)
                gather(step, g)

            load_index(0, 0)
            load_index(1, 1)
            load_gather_index(0, 0)
            load_gather_index(0, 1)
            split_index(0, 0, 0)
            split_index(1, 1, 0)
            rows(0, 0, 2)
            batch(0, 0, 2, (2, 0), 2 * G)

            def beside(u, last):
                left = G if last else 2 * G
                for i in range(2):
                    t = u * 2 + i
                    batch(u, 2 * i + 1, t + 2, None if last and i else (t + 3, 1 - i), left)
                    if 2 * i + 2 < left:
                        batch(*((u, 2) if i == 0 else (u + 1, 0)), left=left if i == 0 else G)
                    split_index(t + 2, i, u + 1)

            with pool.Fori(0, STEPS - 1) as u:
                beside(u, False)
            beside(STEPS - 1, True)

        @block.vector
        def _(dve):
            def onehots(t, i, n):
                k, c = divmod(n, NC)
                q0, m = CHUNKS[c]
                if n == 0:
                    dve.wait_ge(index_split, t * 2 + 2)
                if n >= NBUF or not isinstance(t, int) or t >= 1:
                    dve.wait_ge(group_ready, t * GT + groups_before(*divmod(n - NBUF + 1, NC)))
                col = k * PAIRS + q0
                for dst, src, w in ((oh_hi[n % NBUF], hi2[i], P), (oh_lo[n % NBUF], lo2[i], ROWS)):
                    shape = [P, m, w // 2, 2]
                    last = nc.vector.tensor_tensor(
                        dst[:, 0:m, :].rearrange("p m (w two) -> p m w two", two=2),
                        src[:, col:col + m, :].unsqueeze(2).broadcast_to(shape),
                        ramp[:, 0:w].rearrange("p (w two) -> p w two", two=2).unsqueeze(1).broadcast_to(shape),
                        ALU.is_equal)
                last.then_inc(onehot_ready, 1)

            def residual(t, i, x, turn):
                if x == 0:
                    dve.wait_ge(table_loaded[i], turn * LOADS + LOADS)
                w = slice(x * PW, (x + 1) * PW)
                nc.vector.tensor_tensor(res[i][:, w], tab[i][:, w], halves[i][:, w, 1], ALU.subtract
                                        ).then_inc(residual_ready, 1)

            def last_part(t, i, x):
                w = slice(x * PW, (x + 1) * PW)
                r = slice(W + 1 + x * PW, W + 1 + (x + 1) * PW)
                lo = slice(SHIFT + x * PW, SHIFT + (x + 1) * PW)
                dve.wait_ge(residual_ready, t * PIECES + PIECES)
                if x > 0:
                    dve.wait_ge(parts_ready, t * PIECES + x)
                nc.vector.tensor_tensor(halves[i][:, lo, 0], res[i][:, w], halves[i][:, r, 1], ALU.subtract
                                        ).then_inc(parts_ready, 1)

            def pool_slot(t, i, k):
                if k == 0:
                    dve.wait_ge(stage_free, t + 1)
                s = t * NSLOT + k
                dve.wait_ge(slot_done, s + 1)
                nc.vector.tensor_reduce(stage[:, k, i, :],
                                        ps_acc[k % 2][:, 0:3 * E].rearrange("p (h e) -> p e h", h=3),
                                        AX.X, ALU.add).then_inc(acc_free, 1)

            def sum_gathered(step, g):
                h = g % 2
                n = step * G + g
                dve.wait_ge(gathered[h], step * (8 * G * GN) + (g // 2 + 1) * (16 * GN))
                nc.vector.tensor_reduce(g_sum[h][:, :, :], g_buf[h][:, :, :, :].rearrange("p s j e -> p s e j"),
                                        AX.X, ALU.add).then_inc(g_free, 1)
                dve.wait_ge(g_free, n + 3)
                nc.vector.tensor_tensor(g_pool[:, g // 2, :, h, :], g_pool[:, g // 2, :, h, :], g_sum[h][:, :, :], ALU.add
                                        ).then_inc(g_added, 1)

            def table(t, i, turn_next, last, step):
                for k in range(NSLOT):
                    for p in range(NC):
                        if step is not None and (k, p) in SUM_AT:
                            sum_gathered(step, 2 * i + SUM_AT[k, p])
                        n = (k + 1) * NC + AHEAD + p
                        if not last and (k, p) in RES_AT:
                            residual(t + 1, 1 - i, RES_AT[k, p], turn_next)
                        if n < CT:
                            onehots(t, i, n)
                        elif not last:
                            onehots(t + 1, 1 - i, n - CT)
                        if not last and (k, p) in LO_AT:
                            last_part(t + 1, 1 - i, LO_AT[k, p])
                    if last and k == NSLOT - 1:
                        for x in range(1, len(EARLY), 2):
                            dve.wait_ge(feat_ready, x + 1)
                            nc.vector.tensor_copy(feat[EARLY[x]], ps_mlp[1][:, :]).then_inc(feat_used[1], 1)
                    pool_slot(t, i, k)

            for buffers_free in (acc_free, stage_free, g_free):
                dve.sem_inc(buffers_free, 2)
            for i in range(2):
                nc.vector.memset(tab[i][96:P, LAST * E:], 0.0).then_inc(tails_zero, 1)
            nc.vector.memset(g_pool[:, :, :, :, :], 0.0).then_inc(g_added, 1)
            dve.wait_ge(g_added, 1)
            dve.wait_ge(constants, 1)
            for n in range(NBUF):
                onehots(0, 0, n)
            for x in range(PIECES):
                residual(0, 0, x, 0)
            for x in range(PIECES):
                if NBUF + x < NC + AHEAD:
                    onehots(0, 0, NBUF + x)
                last_part(0, 0, x)
            dve.wait_ge(mlp_used, KH + 1)
            with dve.Fori(0, LOOPS) as u:
                table(u * 2, 0, u, False, u)
                table(u * 2 + 1, 1, u + 1, False, u)
            table(T - 2, 0, LOOPS, False, None)
            table(T - 1, 1, None, True, None)

        @block.scalar
        def _(act):
            def copy_counts(t, n):
                k, g = divmod(n, NG)
                q0, m = GROUPS[g]
                out = counts[k % 2][:, :].rearrange("p (h x) -> p h x", h=2)
                act.wait_ge(group_ready, t * GT + n + 1)
                nc.scalar.activation(out[:, :, q0 * ROWS:(q0 + m) * ROWS], ps_cnt[n % 2][:, :, 0:m * ROWS],
                                     ACT.Copy).then_inc(counts_ready, 1)

            def relu(dst, ps, bias, n):
                act.wait_ge(mlp_ready, n)
                nc.scalar.activation(dst, ps, ACT.Relu, bias=bias).then_inc(mlp_used, 1)

            def table(t, last):
                for n in range(NG, GT):
                    copy_counts(t, n)
                if not last:
                    for n in range(NG):
                        copy_counts(t + 1, n)

            act.wait_ge(dense_loaded, 8 * 16)
            for m in range(KH):
                relu(h_d[:, m, :], ps_mlp[m % 2][:, :], b_d1[:, m:m + 1], m + 1)
            relu(dense_x[:, :], ps_mlp[KH % 2][0:E, :], b_d2[:, :], KH + 1)
            for n in range(NG):
                copy_counts(0, n)
            with act.Fori(0, LOOPS) as u:
                table(u * 2, False)
                table(u * 2 + 1, False)
            table(T - 2, False)
            table(T - 1, True)
            for x in range(0, KF, 2):
                act.wait_ge(feat_ready, x + 1)
                nc.scalar.activation(feat[(EARLY + [LATE])[x]], ps_mlp[0][:, :], ACT.Copy).then_inc(feat_used[0], 1)
            for m in range(KH):
                relu(h_o[:, m, :], ps_cnt[m // 2][:, m % 2, :], b_o1[:, m:m + 1], KH + 1 + m + 1)
            for h in range(2):
                relu(out_row[h], ps_acc[0][0:1, h * (B // 2):(h + 1) * (B // 2)], b_o2[:, :], 2 * KH + 2)

        @block.tensor
        def _(pe):
            def count_group(t, n):
                k, g = divmod(n, NG)
                q0, m = GROUPS[g]
                c = g // 2
                ch = k * NC + c
                pe.wait_ge(onehot_ready, t * CT + ch + 1)
                if n >= 2 or not isinstance(t, int) or t >= 1:
                    pe.wait_ge(counts_ready, t * GT + n - 1)
                for q in range(m):
                    for h in range(2):
                        j = slice(h * HALF, h * HALF + BAG)
                        x = q0 + q - CHUNKS[c][0]
                        last = nc.tensor.matmul(ps_cnt[n % 2][:, h, q * ROWS:(q + 1) * ROWS],
                                                oh_hi[ch % NBUF][j, x, :], oh_lo[ch % NBUF][j, x, :],
                                                start=True, stop=True)
                last.then_inc(group_ready, 1)

            def accumulate(t, i, k, l0, l1):
                acc = ps_acc[k % 2]
                cnt = counts[k % 2][:, :].rearrange("p (b l) -> p b l", l=ROWS)
                if k == 0 and -(-l1 // PL) > -(-l0 // PL):
                    pe.wait_ge(parts_ready, t * PIECES + -(-l1 // PL))
                if l0 == 0:
                    pe.wait_ge(counts_ready, t * GT + (k + 1) * NG)
                    pe.wait_ge(acc_free, t * NSLOT + k + 1)
                for l in range(l0, l1):
                    last = nc.tensor.matmul(acc[:, 0:3 * E], cnt[:, :, l], three_parts(i, l),
                                            start=(l == 0), stop=(l == ROWS - 1))
                if l1 == ROWS:
                    last.then_inc(slot_done, 1)

            def transpose_features(x):
                k = (EARLY + [LATE])[x]
                if x == 0:
                    pe.wait_ge(back_loaded, 16)
                    pe.wait_ge(g_added, STEPS * G + 1)
                    pe.wait_ge(constants, 3)
                    pe.wait_ge(mlp_used, KH + 1)
                if k == LATE:
                    pe.wait_ge(acc_free, T * NSLOT + 2)
                if x >= 2:
                    pe.wait_ge(feat_used[x % 2], x // 2)
                for s in range(NSLOT):
                    last = nc.tensor.transpose(ps_mlp[x % 2][:, s * P:(s + 1) * P], sums(k, s), ident[:, :])
                last.then_inc(feat_ready, 1)

            def table(t, i, last):
                for k in range(NSLOT):
                    for g in range(NG):
                        n = (k + 1) * NG + g
                        if n < GT:
                            count_group(t, n)
                        elif not last:
                            count_group(t + 1, n - GT)
                        elif g < len(EARLY):
                            transpose_features(g)
                        accumulate(t, i, k, g * ROWS // NG, (g + 1) * ROWS // NG)

            def product(ps, pairs, start=True, stop=True):
                for k, (lhs, rhs) in enumerate(pairs):
                    last = nc.tensor.matmul(ps, lhs, rhs, start=(start and k == 0), stop=(stop and k == len(pairs) - 1))
                if stop:
                    last.then_inc(mlp_ready, 1)

            pe.wait_ge(dense_loaded, 8 * 16)
            for m in range(KH):
                if m >= 2:
                    pe.wait_ge(mlp_used, m - 1)
                product(ps_mlp[m % 2][:, :], [(w_d1[:, k, m * P:(m + 1) * P], xT[:, k, :]) for k in range(KD)])
            pe.wait_ge(mlp_used, KH)
            product(ps_mlp[KH % 2][0:E, :], [(w_d2[:, k, :], h_d[:, k, :]) for k in range(KH)])
            for n in range(NG):
                count_group(0, n)
            with pe.Fori(0, LOOPS) as u:
                table(u * 2, 0, False)
                table(u * 2 + 1, 1, False)
            table(T - 2, 0, False)
            table(T - 1, 1, True)

            pe.wait_ge(weights_loaded, 3 * 16)
            pe.wait_ge(counts_ready, T * GT)
            pe.wait_ge(feat_used[0], len(EARLY) // 2)
            pe.wait_ge(feat_used[1], len(EARLY) // 2)
            for m in range(KH):
                c = slice(m * P, (m + 1) * P)
                ps = ps_cnt[m // 2][:, m % 2, :]
                product(ps, [(w_dense[:, c], dense_x[:, :])] + [(w_feat[k][:, c], feat[k]) for k in EARLY],
                        stop=False)
                if m == 0:
                    transpose_features(len(EARLY))
                    pe.wait_ge(feat_used[0], len(EARLY) // 2 + 1)
                product(ps, [(w_feat[LATE][:, c], feat[LATE])], start=False)
            pe.wait_ge(mlp_used, 2 * KH + 1)
            product(ps_acc[0][0:1, :], [(w_o2[:, k:k + 1], h_o[:, k, :]) for k in range(KH)])


def kernel(r_dense_features, r_sparse_features, L0_rec_emb_tables, L0_rec_d_w1, L0_rec_d_b1, L0_rec_d_w2,
           L0_rec_d_b2, L0_rec_o_w1, L0_rec_o_b1, L0_rec_o_w2, L0_rec_o_b2):
    import concourse.bacc as bacc
    import numpy as np
    from concourse.bass_utils import run_bass_kernel_spmd

    a = np.asarray
    sparse = a(r_sparse_features)
    tables, batch, bag = sparse.shape
    by_pair = sparse.reshape(tables, batch // 128, 2, 64, bag).transpose(0, 2, 4, 1, 3)
    by_pair = np.pad(by_pair, ((0, 0), (0, 0), (0, 64 - bag), (0, 0), (0, 0)))
    gathered, steps = 4, 10
    by_step = sparse[tables - gathered:].reshape(gathered, batch // 128, 128, steps, bag // steps)
    by_step = by_step.transpose(3, 0, 2, 1, 4).reshape(steps, gathered, 128, -1)
    arrays = {
        "dense_T": a(r_dense_features).T,
        "bag_index": by_pair.reshape(tables, 128, batch // 2),
        "gather_index": by_step,
        "tables": a(L0_rec_emb_tables),
        "d_w1T": a(L0_rec_d_w1).T,
        "d_b1": a(L0_rec_d_b1),
        "d_w2T": a(L0_rec_d_w2).T,
        "d_b2": a(L0_rec_d_b2),
        "o_w1T": a(L0_rec_o_w1).T,
        "o_b1": a(L0_rec_o_b1),
        "o_w2T": a(L0_rec_o_w2).T,
        "o_b2": a(L0_rec_o_b2),
    }
    arrays = {n: np.ascontiguousarray(x) for n, x in arrays.items()}
    nc = bacc.Bacc("TRN2", target_bir_lowering=False, num_devices=1)
    args = [nc.dram_tensor(n, x.shape, mybir.dt.from_np(x.dtype), kind="ExternalInput").ap()
            for n, x in arrays.items()]
    out = nc.dram_tensor("logits", (batch, 1), mybir.dt.float32, kind="ExternalOutput").ap()
    embedding_bag_mlp_program(nc, *args, out)
    r = run_bass_kernel_spmd(nc, [arrays], core_ids=[0])
    return r.results[0]["logits"]
```

```python
from contextlib import ExitStack

import concourse.bass as bass
from concourse import mybir


def embedding_bag_mlp_program(nc, dense_T, bag_index, gather_index, rest_index, tables, d_w1T, d_b1, d_w2T, d_b2,
                              o_w1T, o_b1, o_w2T, o_b2, logits):
    fp32, bf16, i32 = mybir.dt.float32, mybir.dt.bfloat16, mybir.dt.int32
    ALU = mybir.AluOpType
    ACT = mybir.ActivationFunctionType
    AX = mybir.AxisListType

    P = 128
    ALL, V, E = tables.shape
    STEPS, G, _, GN = gather_index.shape
    T = ALL - G
    RB = rest_index.shape[0]
    DD, B = dense_T.shape
    HID = o_w1T.shape[1]
    BAG = 50
    ROWS = -(-V // P)
    LAST = V - (P - 1) * ROWS
    HALF = P // 2
    SLOT = P
    NSLOT = B // SLOT
    PAIRS = SLOT // 2
    GROUP = 512 // ROWS
    CHUNK = 2 * GROUP
    GROUPS = [(q, min(GROUP, PAIRS - q)) for q in range(0, PAIRS, GROUP)]
    CHUNKS = [(q, min(CHUNK, PAIRS - q)) for q in range(0, PAIRS, CHUNK)]
    NC, NG = len(CHUNKS), len(GROUPS)
    NBUF = 4
    AHEAD = 3
    PIECES = 7
    W = ROWS * E
    PL = ROWS // PIECES
    PW = PL * E
    RES_AT = {(1, 0): 0, (1, 1): 1, (1, 3): 2, (1, 4): 3, (1, 6): 4, (2, 0): 5, (2, 2): 6}
    LO_AT = {(2, 3): 0, (2, 5): 1, (2, 6): 2, (3, 1): 3, (3, 2): 4, (3, 4): 5, (3, 5): 6}
    SUM_AT = {(1, 0): 0, (3, 0): 1}
    REST_AT = {(0, 0, 5): 0, (0, 1, 2): 1, (0, 2, 3): 2, (1, 0, 0): 3}
    MAGIC = 1.5 * 2.0 ** 23
    KD, KH, KF = DD // P, HID // P, ALL * E // P
    GJ = GN // NSLOT
    RJ = BAG // RB
    RS = GN // RJ
    KL = NSLOT - RS
    N0 = STEPS * G
    assert ROWS % PIECES == 0 and T % 2 == 0 and NSLOT % 2 == 0 and NSLOT * NC % NBUF == 0
    assert NSLOT * NG % 2 == 0 and BAG <= HALF
    assert N0 % 4 == 0 and KL == 2 and RB == len(REST_AT) + 1 and RB * RJ == BAG
    assert G == 4 and STEPS * GJ == BAG and STEPS == T // 2 - 1

    ctx = ExitStack()
    with ctx:
        def sb(name, shape, dt):
            return ctx.enter_context(nc.sbuf_tensor(name, shape, dt))

        def pb(name, shape, dt=fp32):
            return ctx.enter_context(nc.psum_tensor(name, shape, dt))

        def sem(name):
            return ctx.enter_context(nc.semaphore(name))

        both = [sb(f"table_and_residual{i}", [P, 2 * W + 1], fp32) for i in range(2)]
        counts = [sb(f"counts{i}", [P, SLOT * ROWS], bf16) for i in range(2)]
        oh_hi = [sb(f"onehot_hi{i}", [P, CHUNK, P], bf16) for i in range(NBUF)]
        oh_lo = [sb(f"onehot_lo{i}", [P, CHUNK, ROWS], bf16) for i in range(NBUF)]
        stage = sb("pooled_stage", [P, NSLOT, 2, E], fp32)
        g_pool = sb("gathered_pooled", [P, G // 2, NSLOT, 2, E], fp32)
        w_x = sb("weight_o1_rest", [P, 2, HID], fp32)
        idx = [sb(f"bag_index{i}", [P, B // 2], fp32) for i in range(2)]
        hi2 = [sb(f"hi_twice{i}", [P, B // 2, 2], bf16) for i in range(2)]
        lo2 = [sb(f"lo_twice{i}", [P, B // 2, 2], bf16) for i in range(2)]
        quot, hi_f = (sb(n, [P, B // 2], fp32) for n in ("quotient", "hi_float"))
        step_const = sb("step_constants", [P, 5], fp32)
        g_raw = [sb(f"gather_index{i}", [P, GN], i32) for i in range(2)]
        g_row = [sb(f"gather_row{i}", [P, GN], i32) for i in range(G)]
        g_base = sb("gather_base", [P, 1 + G, GN], i32)
        g_buf = [sb(f"gathered_rows{i}", [P, NSLOT, GJ, E], fp32) for i in range(2)]
        g_sum = [sb(f"gathered_sum{i}", [P, NSLOT, E], fp32) for i in range(2)]
        ramp = sb("ramp", [P, P], bf16)
        ident = sb("ident", [P, P], fp32)
        dense_x = sb("dense_x", [E, B], fp32)
        b_d1 = sb("bias_d1", [P, KH], fp32)
        b_d2 = sb("bias_d2", [E, 1], fp32)
        b_o1 = sb("bias_o1", [P, KH], fp32)
        b_o2 = sb("bias_o2", [1, 1], fp32)
        w_o2 = sb("weight_o2", [P, KH], fp32)
        out_row = hi_f[0:1, :], quot[0:1, :]

        tab = [x[:, 0:W] for x in both]
        res = [x[:, W + 1:2 * W + 1] for x in both]
        halves = [x[:, :].bitcast(bf16).rearrange("p (w h) -> p w h", h=2) for x in both]
        SHIFT = W // 2 + 1

        def three_parts(i, l):
            flat = both[i][:, :].bitcast(bf16)
            return bass.AP(flat.tensor, flat.offset + 2 * l * E + 1, [list(flat.ap[0]), [W + 1, 3], [2, E]])
        spill = nc.dram_tensor("pooled_spill", (T // 2 - 1, P, NSLOT, 2, E), fp32).ap()

        xT = res[1][:, 0:KD * B].rearrange("p (k n) -> p k n", k=KD)
        w_d1 = res[1][:, KD * B:KD * (B + HID)].rearrange("p (k n) -> p k n", k=KD)
        w_d2 = res[1][:, KD * (B + HID):KD * (B + HID) + KH * E].rearrange("p (k n) -> p k n", k=KH)
        h_d = counts[1][:, :].bitcast(fp32)[:, 0:KH * B].rearrange("p (k n) -> p k n", k=KH)
        back = tab[0][:, 0:(T - 2) * NSLOT * E].rearrange("p (u s e) -> p u s e", u=T // 2 - 1, s=NSLOT)
        KW = (ROWS * E) // HID
        w_a = res[0][:, 0:KW * HID].rearrange("p (k n) -> p k n", k=KW)
        h_o = res[1][:, 0:KH * B].rearrange("p (k n) -> p k n", k=KH)
        w_feat = [w_a[:, k, :] if k < KW else w_x[:, k - KW, :] for k in range(KF)]
        w_dense = w_x[0:E, KF - KW, :]
        LATE = T // 2 - 1
        EARLY = [k for k in range(KF) if k != LATE]
        feat = {k: counts[0][:, :].bitcast(fp32)[:, x * B:(x + 1) * B] for x, k in enumerate(EARLY)}
        feat[LATE] = counts[1][:, :].bitcast(fp32)[:, 0:B]
        assert KF - KW == 1 and len(EARLY) * B <= ROWS * E and len(EARLY) < NG

        def sums(k, s):
            if k < LATE:
                return back[:, k, s, :]
            pair = stage[:, s, :, :] if k == LATE else g_pool[:, k - LATE - 1, s, :, :]
            return pair.rearrange("p t e -> p (t e)")

        ps_cnt = [pb(f"ps_counts{i}", [P, 2, 512]) for i in range(2)]
        ps_acc = [pb(f"ps_pooled{i}", [P, 512]) for i in range(2)]
        ps_mlp = [pb(f"ps_mlp{i}", [P, 512]) for i in range(2)]

        constants = sem("constants")
        tails_zero = sem("tails_zero")
        table_loaded = [sem(f"table_loaded{i}") for i in range(2)]
        index_loaded = [sem(f"index_loaded{i}") for i in range(2)]
        index_steps = sem("index_steps")
        index_split = sem("index_split")
        onehot_ready = sem("onehot_ready")
        group_ready = sem("group_ready")
        counts_ready = sem("counts_ready")
        residual_ready = sem("residual_ready")
        parts_ready = sem("parts_ready")
        slot_done = sem("slot_done")
        acc_free = sem("acc_free")
        g_loaded = [sem(f"gather_index_loaded{i}") for i in range(2)]
        gathered = [sem(f"gathered{i}") for i in range(2)]
        rows_ready = sem("rows_ready")
        g_free = sem("gather_buffer_free")
        g_added = sem("gather_added")
        rest_added = sem("rest_added")
        spilled = sem("spilled")
        stage_free = sem("stage_free")
        back_loaded = sem("sums_loaded_back")
        layer1_loaded = sem("layer1_loaded")
        dense_loaded = sem("dense_loaded")
        weights_loaded = sem("weights_loaded")
        mlp_ready = sem("mlp_ready")
        mlp_used = sem("mlp_used")
        feat_ready = sem("feat_ready")
        feat_used = [sem(f"feat_used{i}") for i in range(2)]
        out_stored = sem("out_stored")

        GT, CT = NSLOT * NG, NSLOT * NC
        LOADS = 3 * 16
        LOOPS = T // 2 - 1

        def groups_before(s, c):
            return s * NG + min(2 * c, NG)

        block = ctx.enter_context(nc.Block())

        @block.sync
        def _(sp):
            def load_table(t, i):
                for p0, p1 in ((0, 112), (112, P - 1)):
                    sp.dma_start(tab[i][p0:p1, :],
                                 tables[t, p0 * ROWS:p1 * ROWS, :].rearrange("(p r) e -> p (r e)", r=ROWS)
                                 ).then_inc(table_loaded[i], 16)
                sp.dma_start(tab[i][P - 1:P, 0:LAST * E],
                             tables[t, (P - 1) * ROWS:V, :].rearrange("(p r) e -> p (r e)", p=1)
                             ).then_inc(table_loaded[i], 16)

            with nc.allow_non_contiguous_dma(reason="bias columns, once"):
                for dst, src in ((xT, dense_T), (w_d1, d_w1T)):
                    sp.dma_start(dst, src.rearrange("(k p) n -> p k n", p=P)).then_inc(layer1_loaded, 16)
                for dst, src in ((w_d2, d_w2T.rearrange("(k p) n -> p k n", p=P)),
                                 (b_d1[:, :], d_b1.rearrange("(k p) -> p k", p=P)),
                                 (b_d2[:, :], d_b2.rearrange("(p n) -> p n", n=1)),
                                 (b_o1[:, :], o_b1.rearrange("(k p) -> p k", p=P)),
                                 (b_o2[:, :], o_b2.rearrange("(p n) -> p n", n=1)),
                                 (w_o2[:, :], o_w2T.rearrange("(k p) n -> p (k n)", p=P))):
                    sp.dma_start(dst, src).then_inc(dense_loaded, 16)

            for i in range(2):
                sp.wait_ge(tails_zero, i + 1)
                load_table(i, i)
            for dst, src in ((w_x[:, 0, :], o_w1T[E + KW * P:, :]), (w_dense, o_w1T[0:E, :])):
                sp.dma_start(dst, src).then_inc(weights_loaded, 16)

            def spill_sums(u, i):
                t = u * 2 + i
                sp.wait_ge(acc_free, t * NSLOT + (NSLOT + 2))
                sp.dma_start(spill[u, :, :, i, :], stage[:, :, i, :]).then_inc(spilled, 16)
                sp.wait_ge(spilled, t * 16 + 16)
                sp.sem_inc(stage_free, 1)

            with sp.Fori(0, LOOPS) as u:
                sp.wait_ge(slot_done, u * (2 * NSLOT) + NSLOT)
                load_table(u * 2 + 2, 0)
                spill_sums(u, 0)
                sp.wait_ge(slot_done, u * (2 * NSLOT) + 2 * NSLOT)
                load_table(u * 2 + 3, 1)
                spill_sums(u, 1)
            sp.wait_ge(slot_done, (T - 1) * NSLOT)
            sp.dma_start(back.rearrange("p u s e -> p u (s e)"), spill.rearrange("u p s t e -> p u (s t e)")
                         ).then_inc(back_loaded, 16)
            sp.dma_start(w_a, o_w1T[E:E + KW * P, :].rearrange("(k p) n -> p k n", p=P)).then_inc(weights_loaded, 16)
            sp.wait_ge(mlp_used, 2 * KH + 3)
            for h in range(2):
                sp.dma_start(logits[h * (B // 2):(h + 1) * (B // 2), :].rearrange("b n -> n b"), out_row[h]
                             ).then_inc(out_stored, 16)
            sp.wait_ge(out_stored, 32)

        @block.gpsimd
        def _(pool):
            nc.gpsimd.iota(ramp[:, :], pattern=[[1, P]], base=0, channel_multiplier=0,
                           allow_small_or_imprecise_dtypes=True).then_inc(constants, 1)
            nc.gpsimd.memset(ident[:, :], 0.0).then_inc(constants, 1)
            pool.wait_ge(constants, 2)
            nc.gpsimd.affine_select(out=ident[:, :], in_=ident[:, :], compare_op=ALU.not_equal, fill=1.0,
                                    base=0, pattern=[[-1, P]], channel_multiplier=1).then_inc(constants, 1)

            for c, v in enumerate((-(ROWS - 1) / 2.0, 1.0 / ROWS, MAGIC, -MAGIC, -float(ROWS))):
                nc.gpsimd.memset(step_const[:, c:c + 1], v)
            nc.gpsimd.iota(g_base[:, :, :], pattern=[[V, 1 + G], [0, GN]], base=(T - 1) * V, channel_multiplier=0)
            pool.drain()

            def load_index(t, i):
                pool.dma_start(idx[i][:, :], bag_index[t, :, :]).then_inc(index_loaded[i], 16)

            def split_index(t, i, turn):
                one, two = [P, B // 2], [P, B // 2, 2]
                pool.wait_ge(index_loaded[i], turn * 16 + 16)
                if not (isinstance(t, int) and t < 1):
                    pool.wait_ge(index_split, t * 2)
                src, n = idx[i], t * 5
                for c, (dst, op) in enumerate(((quot, ALU.add), (hi_f, ALU.mult), (quot, ALU.add),
                                               (hi_f, ALU.add), (quot, ALU.mult))):
                    if c > 0:
                        pool.wait_ge(index_steps, n + c)
                    nc.gpsimd.tensor_tensor(dst[:, :], src[:, :], step_const[:, c:c + 1].broadcast_to(one), op
                                            ).then_inc(index_steps, 1)
                    src = dst
                if not (isinstance(t, int) and t < 2):
                    pool.wait_ge(onehot_ready, t * CT - CT)
                pool.wait_ge(index_steps, n + 5)
                nc.gpsimd.tensor_tensor(lo2[i][:, :, :], idx[i][:, :].unsqueeze(2).broadcast_to(two),
                                        quot[:, :].unsqueeze(2).broadcast_to(two), ALU.add
                                        ).then_inc(index_split, 1)
                nc.gpsimd.tensor_copy(hi2[i][:, :, :], hi_f[:, :].unsqueeze(2).broadcast_to(two)
                                      ).then_inc(index_split, 1)

            def load_gather_index(step, g):
                pool.dma_start(g_raw[g % 2][:, :], gather_index[step, g, :, :]).then_inc(g_loaded[g % 2], 16)

            def rows(step, g, tables_split):
                step, g = (step, g) if g < G else (step + 1, g - G)
                n = step * G + g
                if tables_split is not None:
                    pool.wait_ge(index_split, tables_split * 2)
                if not (isinstance(step, int) and n == 0):
                    pool.wait_ge(rows_ready, n)
                    pool.wait_ge(g_free, n)
                pool.wait_ge(g_loaded[g % 2], step * (8 * G) + (g // 2 + 1) * 16)
                nc.gpsimd.tensor_tensor(g_row[g][:, :], g_raw[g % 2][:, :], g_base[:, 1 + g, :], ALU.add
                                        ).then_inc(rows_ready, 1)

            def gather(step, g):
                h = g % 2
                for x in range(GN):
                    s_, j = divmod(x, GJ)
                    nc.gpsimd.indirect_dma_start(g_buf[h][:, s_, j, :], None, tables.rearrange("t v e -> (t v) e"),
                                                 bass.IndirectOffsetOnAxis(g_row[g][:, x:x + 1], 0)
                                                 ).then_inc(gathered[h], 16)

            def load_rest_index(x):
                pool.dma_start(g_raw[x % 2][:, :], rest_index[x, :, :]).then_inc(g_loaded[x % 2], 16)

            def rest_rows(x):
                n = N0 + x
                pool.wait_ge(rows_ready, n)
                pool.wait_ge(g_free, n)
                pool.wait_ge(g_loaded[x % 2], (N0 // 2 + x // 2 + 1) * 16)
                nc.gpsimd.tensor_tensor(g_row[x % G][:, :], g_raw[x % 2][:, :], g_base[:, 0, :], ALU.add
                                        ).then_inc(rows_ready, 1)

            def rest_batch(x):
                if x + 1 < RB:
                    rest_rows(x + 1)
                else:
                    pool.wait_ge(rows_ready, N0 + RB)
                    pool.wait_ge(g_free, N0 + RB)
                if x + 2 < RB:
                    load_rest_index(x + 2)
                buf = g_buf[x % 2][:, :, :, :].rearrange("p s j e -> p (s j) e")
                for c in range(GN):
                    nc.gpsimd.indirect_dma_start(buf[:, c, :], None, tables.rearrange("t v e -> (t v) e"),
                                                 bass.IndirectOffsetOnAxis(g_row[x % G][:, c:c + 1], 0)
                                                 ).then_inc(gathered[x % 2], 16)

            def batch(step, g, tables_split=None, index=None, left=2 * G):
                if g + 1 < left:
                    rows(step, g + 1, tables_split)
                else:
                    rest_rows(0)
                if g + 2 < left:
                    load_gather_index(*((step, g + 2) if g + 2 < G else (step + 1, g + 2 - G)))
                else:
                    load_rest_index(g + 2 - left)
                if index is not None:
                    load_index(*index)
                gather(step, g)

            load_index(0, 0)
            load_index(1, 1)
            load_gather_index(0, 0)
            load_gather_index(0, 1)
            split_index(0, 0, 0)
            split_index(1, 1, 0)
            rows(0, 0, 2)
            batch(0, 0, 2, (2, 0))

            def beside(u, last):
                left = G if last else 2 * G
                for i in range(2):
                    t = u * 2 + i
                    batch(u, 2 * i + 1, t + 2, None if last and i else (t + 3, 1 - i), left)
                    if 2 * i + 2 < left:
                        batch(*((u, 2) if i == 0 else (u + 1, 0)), left=left if i == 0 else 2 * G)
                    if last and i == 1:
                        rest_batch(0)
                    split_index(t + 2, i, u + 1)

            with pool.Fori(0, STEPS - 1) as u:
                beside(u, False)
            beside(STEPS - 1, True)
            for x in range(1, RB):
                rest_batch(x)

        @block.vector
        def _(dve):
            def onehots(t, i, n):
                k, c = divmod(n, NC)
                q0, m = CHUNKS[c]
                if n == 0:
                    dve.wait_ge(index_split, t * 2 + 2)
                if n >= NBUF or not isinstance(t, int) or t >= 1:
                    dve.wait_ge(group_ready, t * GT + groups_before(*divmod(n - NBUF + 1, NC)))
                col = k * PAIRS + q0
                for dst, src, w in ((oh_hi[n % NBUF], hi2[i], P), (oh_lo[n % NBUF], lo2[i], ROWS)):
                    shape = [P, m, w // 2, 2]
                    last = nc.vector.tensor_tensor(
                        dst[:, 0:m, :].rearrange("p m (w two) -> p m w two", two=2),
                        src[:, col:col + m, :].unsqueeze(2).broadcast_to(shape),
                        ramp[:, 0:w].rearrange("p (w two) -> p w two", two=2).unsqueeze(1).broadcast_to(shape),
                        ALU.is_equal)
                last.then_inc(onehot_ready, 1)

            def residual(t, i, x, turn):
                if x == 0:
                    dve.wait_ge(table_loaded[i], turn * LOADS + LOADS)
                w = slice(x * PW, (x + 1) * PW)
                nc.vector.tensor_tensor(res[i][:, w], tab[i][:, w], halves[i][:, w, 1], ALU.subtract
                                        ).then_inc(residual_ready, 1)

            def last_part(t, i, x):
                w = slice(x * PW, (x + 1) * PW)
                r = slice(W + 1 + x * PW, W + 1 + (x + 1) * PW)
                lo = slice(SHIFT + x * PW, SHIFT + (x + 1) * PW)
                dve.wait_ge(residual_ready, t * PIECES + PIECES)
                if x > 0:
                    dve.wait_ge(parts_ready, t * PIECES + x)
                nc.vector.tensor_tensor(halves[i][:, lo, 0], res[i][:, w], halves[i][:, r, 1], ALU.subtract
                                        ).then_inc(parts_ready, 1)

            def pool_slot(t, i, k):
                if k == 0:
                    dve.wait_ge(stage_free, t + 1)
                s = t * NSLOT + k
                dve.wait_ge(slot_done, s + 1)
                nc.vector.tensor_reduce(stage[:, k, i, :],
                                        ps_acc[k % 2][:, 0:3 * E].rearrange("p (h e) -> p e h", h=3),
                                        AX.X, ALU.add).then_inc(acc_free, 1)

            def sum_gathered(step, g):
                h = g % 2
                n = step * G + g
                dve.wait_ge(gathered[h], step * (8 * G * GN) + (g // 2 + 1) * (16 * GN))
                nc.vector.tensor_reduce(g_sum[h][:, :, :], g_buf[h][:, :, :, :].rearrange("p s j e -> p s e j"),
                                        AX.X, ALU.add).then_inc(g_free, 1)
                dve.wait_ge(g_free, n + 3)
                nc.vector.tensor_tensor(g_pool[:, g // 2, :, h, :], g_pool[:, g // 2, :, h, :], g_sum[h][:, :, :], ALU.add
                                        ).then_inc(g_added, 1)

            def sum_rest(x):
                h = x % 2
                into = stage[:, KL:, 1, :]
                rows_of = g_buf[h][:, :, :, :].rearrange("p s j e -> p (s j) e")
                rows_of = rows_of.rearrange("p (s j) e -> p s e j", s=RS)
                dve.wait_ge(gathered[h], (N0 // 2 + x // 2 + 1) * (16 * GN))
                if x == 0:
                    dve.wait_ge(stage_free, T)
                    nc.vector.tensor_reduce(into, rows_of, AX.X, ALU.add).then_inc(rest_added, 1)
                    dve.wait_ge(rest_added, 1)
                    dve.sem_inc(g_free, 1)
                    return
                nc.vector.tensor_reduce(g_sum[h][:, 0:RS, :], rows_of, AX.X, ALU.add).then_inc(g_free, 1)
                dve.wait_ge(g_free, N0 + x + 3)
                nc.vector.tensor_tensor(into, into, g_sum[h][:, 0:RS, :], ALU.add).then_inc(rest_added, 1)

            def table(t, i, turn_next, last, step):
                for k in range(KL if last else NSLOT):
                    for p in range(NC):
                        if step is None and (i, k, p) in REST_AT:
                            sum_rest(REST_AT[i, k, p])
                        if step is not None and (k, p) in SUM_AT:
                            sum_gathered(step, 2 * i + SUM_AT[k, p])
                        n = (k + 1) * NC + AHEAD + p
                        if not last and (k, p) in RES_AT:
                            residual(t + 1, 1 - i, RES_AT[k, p], turn_next)
                        if n < (KL * NC if last else CT):
                            onehots(t, i, n)
                        elif not last:
                            onehots(t + 1, 1 - i, n - CT)
                        if not last and (k, p) in LO_AT:
                            last_part(t + 1, 1 - i, LO_AT[k, p])
                    if last and k == KL - 1:
                        for x in range(1, len(EARLY), 2):
                            dve.wait_ge(feat_ready, x + 1)
                            nc.vector.tensor_copy(feat[EARLY[x]], ps_mlp[1][:, :]).then_inc(feat_used[1], 1)
                        sum_rest(RB - 1)
                    pool_slot(t, i, k)

            for buffers_free in (acc_free, stage_free, g_free):
                dve.sem_inc(buffers_free, 2)
            for i in range(2):
                nc.vector.memset(tab[i][96:P, LAST * E:], 0.0).then_inc(tails_zero, 1)
            nc.vector.memset(g_pool[:, :, :, :, :], 0.0).then_inc(g_added, 1)
            dve.wait_ge(g_added, 1)
            dve.wait_ge(constants, 1)
            for n in range(NBUF):
                onehots(0, 0, n)
            for x in range(PIECES):
                residual(0, 0, x, 0)
            for x in range(PIECES):
                if NBUF + x < NC + AHEAD:
                    onehots(0, 0, NBUF + x)
                last_part(0, 0, x)
            dve.wait_ge(mlp_used, KH + 1)
            with dve.Fori(0, LOOPS) as u:
                table(u * 2, 0, u, False, u)
                table(u * 2 + 1, 1, u + 1, False, u)
            table(T - 2, 0, LOOPS, False, None)
            table(T - 1, 1, None, True, None)

        @block.scalar
        def _(act):
            def copy_counts(t, n):
                k, g = divmod(n, NG)
                q0, m = GROUPS[g]
                out = counts[k % 2][:, :].rearrange("p (h x) -> p h x", h=2)
                act.wait_ge(group_ready, t * GT + n + 1)
                nc.scalar.activation(out[:, :, q0 * ROWS:(q0 + m) * ROWS], ps_cnt[n % 2][:, :, 0:m * ROWS],
                                     ACT.Copy).then_inc(counts_ready, 1)

            def relu(dst, ps, bias, n):
                act.wait_ge(mlp_ready, n)
                nc.scalar.activation(dst, ps, ACT.Relu, bias=bias).then_inc(mlp_used, 1)

            def table(t, last):
                for n in range(NG, KL * NG if last else GT):
                    copy_counts(t, n)
                if not last:
                    for n in range(NG):
                        copy_counts(t + 1, n)

            act.wait_ge(dense_loaded, 6 * 16)
            for m in range(KH):
                if m == KH - 1:
                    for n in range(2):
                        copy_counts(0, n)
                relu(h_d[:, m, :], ps_mlp[m % 2][:, :], b_d1[:, m:m + 1], m + 1)
            for n in range(2, 3 + KH):
                copy_counts(0, n)
            relu(dense_x[:, :], ps_mlp[KH % 2][0:E, :], b_d2[:, :], KH + 1)
            for n in range(3 + KH, NG):
                copy_counts(0, n)
            with act.Fori(0, LOOPS) as u:
                table(u * 2, False)
                table(u * 2 + 1, False)
            table(T - 2, False)
            table(T - 1, True)
            for x in range(0, KF, 2):
                act.wait_ge(feat_ready, x + 1)
                nc.scalar.activation(feat[(EARLY + [LATE])[x]], ps_mlp[0][:, :], ACT.Copy).then_inc(feat_used[0], 1)
            for m in range(KH):
                relu(h_o[:, m, :], ps_cnt[m // 2][:, m % 2, :], b_o1[:, m:m + 1], KH + 1 + m + 1)
            for h in range(2):
                relu(out_row[h], ps_acc[0][0:1, h * (B // 2):(h + 1) * (B // 2)], b_o2[:, :], 2 * KH + 2)

        @block.tensor
        def _(pe):
            def count_group(t, n):
                k, g = divmod(n, NG)
                q0, m = GROUPS[g]
                c = g // 2
                ch = k * NC + c
                pe.wait_ge(onehot_ready, t * CT + ch + 1)
                if n >= 2 or not isinstance(t, int) or t >= 1:
                    pe.wait_ge(counts_ready, t * GT + n - 1)
                for q in range(m):
                    for h in range(2):
                        j = slice(h * HALF, h * HALF + BAG)
                        x = q0 + q - CHUNKS[c][0]
                        last = nc.tensor.matmul(ps_cnt[n % 2][:, h, q * ROWS:(q + 1) * ROWS],
                                                oh_hi[ch % NBUF][j, x, :], oh_lo[ch % NBUF][j, x, :],
                                                start=True, stop=True)
                last.then_inc(group_ready, 1)

            def accumulate(t, i, k, l0, l1):
                acc = ps_acc[k % 2]
                cnt = counts[k % 2][:, :].rearrange("p (b l) -> p b l", l=ROWS)
                if k == 0 and -(-l1 // PL) > -(-l0 // PL):
                    pe.wait_ge(parts_ready, t * PIECES + -(-l1 // PL))
                if l0 == 0:
                    pe.wait_ge(counts_ready, t * GT + (k + 1) * NG)
                    pe.wait_ge(acc_free, t * NSLOT + k + 1)
                for l in range(l0, l1):
                    last = nc.tensor.matmul(acc[:, 0:3 * E], cnt[:, :, l], three_parts(i, l),
                                            start=(l == 0), stop=(l == ROWS - 1))
                if l1 == ROWS:
                    last.then_inc(slot_done, 1)

            def transpose_features(x):
                k = (EARLY + [LATE])[x]
                if x == 0:
                    pe.wait_ge(back_loaded, 16)
                    pe.wait_ge(g_added, N0 + 1)
                    pe.wait_ge(constants, 3)
                    pe.wait_ge(mlp_used, KH + 1)
                if k == LATE:
                    pe.wait_ge(acc_free, (T - 1) * NSLOT + KL + 2)
                    pe.wait_ge(rest_added, RB)
                if x >= 2:
                    pe.wait_ge(feat_used[x % 2], x // 2)
                for s in range(NSLOT):
                    last = nc.tensor.transpose(ps_mlp[x % 2][:, s * P:(s + 1) * P], sums(k, s), ident[:, :])
                last.then_inc(feat_ready, 1)

            def table(t, i, last):
                for k in range(KL if last else NSLOT):
                    for g in range(NG):
                        n = (k + 1) * NG + g
                        if n < (KL * NG if last else GT):
                            count_group(t, n)
                        elif not last:
                            count_group(t + 1, n - GT)
                        elif g < len(EARLY):
                            transpose_features(g)
                        accumulate(t, i, k, g * ROWS // NG, (g + 1) * ROWS // NG)

            def product(ps, pairs, start=True, stop=True):
                for k, (lhs, rhs) in enumerate(pairs):
                    last = nc.tensor.matmul(ps, lhs, rhs, start=(start and k == 0), stop=(stop and k == len(pairs) - 1))
                if stop:
                    last.then_inc(mlp_ready, 1)

            pe.wait_ge(layer1_loaded, 2 * 16)
            for m in range(KH):
                if m == KH - 1:
                    for n in range(2):
                        count_group(0, n)
                if m >= 2:
                    pe.wait_ge(mlp_used, m - 1)
                product(ps_mlp[m % 2][:, :], [(w_d1[:, k, m * P:(m + 1) * P], xT[:, k, :]) for k in range(KD)])
            for n in range(2, 4):
                count_group(0, n)
            pe.wait_ge(dense_loaded, 6 * 16)
            pe.wait_ge(mlp_used, KH)
            for k in range(KH):
                product(ps_mlp[KH % 2][0:E, :], [(w_d2[:, k, :], h_d[:, k, :])], start=(k == 0), stop=(k == KH - 1))
                count_group(0, 4 + k)
            for n in range(4 + KH, NG):
                count_group(0, n)
            with pe.Fori(0, LOOPS) as u:
                table(u * 2, 0, False)
                table(u * 2 + 1, 1, False)
            table(T - 2, 0, False)
            table(T - 1, 1, True)

            pe.wait_ge(weights_loaded, 3 * 16)
            pe.wait_ge(counts_ready, (T - 1) * GT + KL * NG)
            pe.wait_ge(feat_used[0], len(EARLY) // 2)
            pe.wait_ge(feat_used[1], len(EARLY) // 2)
            for m in range(KH):
                c = slice(m * P, (m + 1) * P)
                ps = ps_cnt[m // 2][:, m % 2, :]
                product(ps, [(w_dense[:, c], dense_x[:, :])] + [(w_feat[k][:, c], feat[k]) for k in EARLY],
                        stop=False)
                if m == 0:
                    transpose_features(len(EARLY))
                    pe.wait_ge(feat_used[0], len(EARLY) // 2 + 1)
                product(ps, [(w_feat[LATE][:, c], feat[LATE])], start=False)
            pe.wait_ge(mlp_used, 2 * KH + 1)
            product(ps_acc[0][0:1, :], [(w_o2[:, k:k + 1], h_o[:, k, :]) for k in range(KH)])


def kernel(r_dense_features, r_sparse_features, L0_rec_emb_tables, L0_rec_d_w1, L0_rec_d_b1, L0_rec_d_w2,
           L0_rec_d_b2, L0_rec_o_w1, L0_rec_o_b1, L0_rec_o_w2, L0_rec_o_b2):
    import concourse.bacc as bacc
    import numpy as np
    from concourse.bass_utils import run_bass_kernel_spmd

    a = np.asarray
    sparse = a(r_sparse_features)
    tables, batch, bag = sparse.shape
    by_pair = sparse.reshape(tables, batch // 128, 2, 64, bag).transpose(0, 2, 4, 1, 3)
    by_pair = np.pad(by_pair, ((0, 0), (0, 0), (0, 64 - bag), (0, 0), (0, 0)))
    gathered, steps = 4, 10
    by_step = sparse[tables - gathered:].reshape(gathered, batch // 128, 128, steps, bag // steps)
    by_step = by_step.transpose(3, 0, 2, 1, 4).reshape(steps, gathered, 128, -1)
    rest, slots = 5, 2
    by_batch = sparse[tables - gathered - 1, batch - 128 * slots:].reshape(slots, 128, rest, bag // rest)
    by_batch = by_batch.transpose(2, 1, 0, 3).reshape(rest, 128, -1)
    arrays = {
        "dense_T": a(r_dense_features).T,
        "bag_index": by_pair.reshape(tables, 128, batch // 2),
        "gather_index": by_step,
        "rest_index": by_batch,
        "tables": a(L0_rec_emb_tables),
        "d_w1T": a(L0_rec_d_w1).T,
        "d_b1": a(L0_rec_d_b1),
        "d_w2T": a(L0_rec_d_w2).T,
        "d_b2": a(L0_rec_d_b2),
        "o_w1T": a(L0_rec_o_w1).T,
        "o_b1": a(L0_rec_o_b1),
        "o_w2T": a(L0_rec_o_w2).T,
        "o_b2": a(L0_rec_o_b2),
    }
    arrays = {n: np.ascontiguousarray(x) for n, x in arrays.items()}
    nc = bacc.Bacc("TRN2", target_bir_lowering=False, num_devices=1)
    args = [nc.dram_tensor(n, x.shape, mybir.dt.from_np(x.dtype), kind="ExternalInput").ap()
            for n, x in arrays.items()]
    out = nc.dram_tensor("logits", (batch, 1), mybir.dt.float32, kind="ExternalOutput").ap()
    embedding_bag_mlp_program(nc, *args, out)
    r = run_bass_kernel_spmd(nc, [arrays], core_ids=[0])
    return r.results[0]["logits"]
```
